# Optimizing a Trainium2 kernel written in Bass

```python
import numpy as np
import jax
import jax.numpy as jnp

def _softmax(x, axis=-1):
    return jax.nn.softmax(x, axis=axis)

def _gelu(x):
    return jax.nn.gelu(x, approximate=True)

def _silu(x):
    return jax.nn.silu(x)

def _sigmoid(x):
    return jax.nn.sigmoid(x)

def _layernorm(x, axis=-1, eps=1e-05):
    m = jnp.mean(x, axis=axis, keepdims=True)
    v = jnp.var(x, axis=axis, keepdims=True)
    return (x - m) / jnp.sqrt(v + eps)

def _scatter_add(tgt, idx, src, axis=0):
    return tgt.at[idx].add(src)

def _segment_sum(src, seg, n):
    return jax.ops.segment_sum(src, seg, n)
kernel_name = 'mk_gps_d1_gnn_r8_198a88'

def setup_inputs(seed: int=0):
    np.random.seed(seed)
    _w = jnp.asarray

    def _rec_inputs():
        import jax
        import jax.numpy as jnp
        _gk = jax.random.key(seed)
        x = -0.0003713 + 1 * jax.random.normal(jax.random.fold_in(_gk, 1), (6250, 256), jnp.float32)
        _s = jax.random.randint(jax.random.fold_in(_gk, 2), (100000,), 0, 6250, jnp.int32)
        _d = jax.random.randint(jax.random.fold_in(_gk, 3), (100000,), 0, 6250, jnp.int32)
        _loop = jnp.arange(6250, dtype=jnp.int32)
        src = jnp.concatenate([_s, _d, _loop])
        dst = jnp.concatenate([_d, _s, _loop])
        _o = jnp.argsort(dst, stable=True)
        src = src[_o]
        dst = dst[_o]
        edge_attr_16 = 0.000196303 + 1.00016 * jax.random.normal(jax.random.fold_in(_gk, 11), (206250, 16), jnp.float32)
        return (x, src, dst, edge_attr_16)
    x, src, dst, edge_attr_16 = _rec_inputs()

    def _L0_gnn_setup():
        import jax, jax.numpy as jnp
        import numpy as np
        N_NODES = 6250
        key = jax.random.key(seed)
        ks = jax.random.split(key, 6)
        d_in, d_out = (256, 256)
        n_edges = 200000
        x = jax.random.normal(ks[0], (N_NODES, d_in), dtype=jnp.float32)
        edge_index = jax.random.randint(ks[1], (2, n_edges), 0, N_NODES, dtype=jnp.int64)
        edge_attr = jax.random.normal(ks[2], (n_edges, 16), dtype=jnp.float32)
        W1 = jax.random.normal(ks[3], (d_in, d_out), dtype=jnp.float32) * (1.0 / np.sqrt(d_in))
        b1 = jnp.zeros((d_out,), dtype=jnp.float32)
        W2 = jax.random.normal(ks[4], (d_out, d_out), dtype=jnp.float32) * (1.0 / np.sqrt(d_out))
        b2 = jnp.zeros((d_out,), dtype=jnp.float32)
        eps = jnp.zeros((1,), dtype=jnp.float32)
        return {'x': x, 'edge_index': edge_index, 'edge_attr': edge_attr, 'W1': W1, 'b1': b1, 'W2': W2, 'b2': b2, 'eps': eps}
    _L0_gnn_all = _L0_gnn_setup()
    _L0_gnn_in = {k: v for k, v in _L0_gnn_all.items() if k in ('W1', 'b1', 'W2', 'b2', 'eps')}
    del _L0_gnn_all

    def _L0_mix_setup():
        import jax, jax.numpy as jnp
        import numpy as np
        NUM_HEADS = 8
        key = jax.random.key(seed)
        ks = jax.random.split(key, 5)
        B, N, C = (8, 2048, 256)
        x = jax.random.normal(ks[0], (B, N, C), dtype=jnp.float32)
        Wq = jax.random.normal(ks[1], (C, C), dtype=jnp.float32) * 0.02
        Wkv = jax.random.normal(ks[2], (2 * C, C), dtype=jnp.float32) * 0.02
        Wproj = jax.random.normal(ks[3], (C, C), dtype=jnp.float32) * 0.02
        bproj = jnp.zeros((C,), dtype=jnp.float32)
        return {'x': x, 'Wq': Wq, 'Wkv': Wkv, 'Wproj': Wproj, 'bproj': bproj}
    _L0_mix_all = _L0_mix_setup()
    _L0_mix_in = {k: v for k, v in _L0_mix_all.items() if k in ('Wq', 'Wkv', 'Wproj', 'bproj')}
    del _L0_mix_all

    def _L0_ffn_setup():
        import jax, jax.numpy as jnp
        import numpy as np
        B, T, D, H, L = (16, 512, 256, 256, 2)

        def _lstm(x, W_ih, W_hh, b_ih, b_hh):
            x_proj = jnp.einsum('btd,gd->btg', x, W_ih) + b_ih + b_hh
            h0 = jnp.zeros((x.shape[0], W_hh.shape[1]), x.dtype)
            c0 = jnp.zeros_like(h0)

            def step(carry, xp):
                h, c = carry
                gates = xp + h @ W_hh.T
                i, f, g, o = jnp.split(gates, 4, axis=-1)
                c = jax.nn.sigmoid(f) * c + jax.nn.sigmoid(i) * jnp.tanh(g)
                h = jax.nn.sigmoid(o) * jnp.tanh(c)
                return ((h, c), h)
            _, hs = jax.lax.scan(step, (h0, c0), jnp.swapaxes(x_proj, 0, 1))
            return jnp.swapaxes(hs, 0, 1)
        key = jax.random.key(seed)
        ks = jax.random.split(key, 9)
        s = 1.0 / np.sqrt(H)
        u = lambda k, shape: jax.random.uniform(k, shape, jnp.float32, -s, s)
        return {'x': jax.random.normal(ks[0], (B, T, D), jnp.float32), 'W_ih': u(ks[1], (4 * H, D)), 'W_hh': u(ks[2], (4 * H, H)), 'b_ih': u(ks[3], (4 * H,)), 'b_hh': u(ks[4], (4 * H,)), 'W_lin': u(ks[5], (L, H)), 'b_lin': u(ks[6], (L,)), 'fw_att': jnp.full((1, H), 0.001, jnp.float32), 'bw_att': jnp.full((1, H), 0.001, jnp.float32)}
    _L0_ffn_all = _L0_ffn_setup()
    _L0_ffn_in = {k: v for k, v in _L0_ffn_all.items() if k in ('W_ih', 'W_hh', 'b_ih', 'b_hh', 'W_lin', 'b_lin', 'fw_att', 'bw_att')}
    del _L0_ffn_all
    return {'x': x, 'src': src, 'dst': dst, 'edge_attr_16': edge_attr_16, 'L0_gnn_W1': _L0_gnn_in['W1'], 'L0_gnn_b1': _L0_gnn_in['b1'], 'L0_gnn_W2': _L0_gnn_in['W2'], 'L0_gnn_b2': _L0_gnn_in['b2'], 'L0_gnn_eps': _L0_gnn_in['eps'], 'L0_mix_Wq': _L0_mix_in['Wq'], 'L0_mix_Wkv': _L0_mix_in['Wkv'], 'L0_mix_Wproj': _L0_mix_in['Wproj'], 'L0_mix_bproj': _L0_mix_in['bproj'], 'L0_ffn_W_ih': _L0_ffn_in['W_ih'], 'L0_ffn_W_hh': _L0_ffn_in['W_hh'], 'L0_ffn_b_ih': _L0_ffn_in['b_ih'], 'L0_ffn_b_hh': _L0_ffn_in['b_hh'], 'L0_ffn_W_lin': _L0_ffn_in['W_lin'], 'L0_ffn_b_lin': _L0_ffn_in['b_lin'], 'L0_ffn_fw_att': _L0_ffn_in['fw_att'], 'L0_ffn_bw_att': _L0_ffn_in['bw_att']}

def reference(x, src, dst, edge_attr_16, L0_gnn_W1, L0_gnn_b1, L0_gnn_W2, L0_gnn_b2, L0_gnn_eps, L0_mix_Wq, L0_mix_Wkv, L0_mix_Wproj, L0_mix_bproj, L0_ffn_W_ih, L0_ffn_W_hh, L0_ffn_b_ih, L0_ffn_b_hh, L0_ffn_W_lin, L0_ffn_b_lin, L0_ffn_fw_att, L0_ffn_bw_att):
    import jax
    import jax.numpy as jnp

    def _L0_gnn_ref(x, edge_index, edge_attr, W1, b1, W2, b2, eps):
        import jax, jax.numpy as jnp
        import numpy as np
        N_NODES = 6250
        src, dst = (edge_index[0], edge_index[1])
        agg = jax.ops.segment_sum(x[src], dst, num_segments=N_NODES)
        h = (1.0 + eps[0]) * x + agg
        h = jax.nn.relu(h @ W1 + b1)
        out = h @ W2 + b2
        return out

    def _L0_mix_ref(x, Wq, Wkv, Wproj, bproj):
        import jax, jax.numpy as jnp
        import numpy as np
        NUM_HEADS = 8
        B, N, C = x.shape
        h = NUM_HEADS
        d = C // h
        q = jnp.einsum('bnc,oc->bno', x, Wq).reshape(B, N, h, d).transpose(0, 2, 1, 3)
        kv = jnp.einsum('bnc,oc->bno', x, Wkv).reshape(B, N, 2, h, d)
        k = kv[:, :, 0].transpose(0, 2, 1, 3)
        v = kv[:, :, 1].transpose(0, 2, 1, 3)
        q = jax.nn.elu(q) + 1.0
        k = jax.nn.elu(k) + 1.0
        k_sum = k.sum(axis=2)
        D_inv = 1.0 / jnp.maximum(jnp.einsum('bhnd,bhd->bhn', q, k_sum), 1e-06)
        context = jnp.einsum('bhnd,bhne->bhde', k, v)
        attn = jnp.einsum('bhnd,bhde->bhne', q, context) * D_inv[..., None]
        out = attn.transpose(0, 2, 1, 3).reshape(B, N, C)
        out = jnp.einsum('bnc,oc->bno', out, Wproj) + bproj
        return out

    def _L0_ffn_ref(x, W_ih, W_hh, b_ih, b_hh, W_lin, b_lin, fw_att, bw_att):
        import jax, jax.numpy as jnp
        import numpy as np
        B, T, D, H, L = (16, 512, 256, 256, 2)

        def _lstm(x, W_ih, W_hh, b_ih, b_hh):
            x_proj = jnp.einsum('btd,gd->btg', x, W_ih) + b_ih + b_hh
            h0 = jnp.zeros((x.shape[0], W_hh.shape[1]), x.dtype)
            c0 = jnp.zeros_like(h0)

            def step(carry, xp):
                h, c = carry
                gates = xp + h @ W_hh.T
                i, f, g, o = jnp.split(gates, 4, axis=-1)
                c = jax.nn.sigmoid(f) * c + jax.nn.sigmoid(i) * jnp.tanh(g)
                h = jax.nn.sigmoid(o) * jnp.tanh(c)
                return ((h, c), h)
            _, hs = jax.lax.scan(step, (h0, c0), jnp.swapaxes(x_proj, 0, 1))
            return jnp.swapaxes(hs, 0, 1)
        lstm_out = _lstm(x, W_ih, W_hh, b_ih, b_hh)
        logits = jnp.einsum('bth,lh->btl', lstm_out, W_lin) + b_lin
        g = jax.lax.stop_gradient(jnp.argmax(logits, axis=-1).astype(lstm_out.dtype))[..., None]
        w = g * lstm_out
        inc = jnp.cumsum(w, axis=1)
        prefix = inc - w
        suffix = inc[:, -1:, :] - inc
        return 2.0 * lstm_out + prefix * fw_att + suffix * bw_att
    edge_index = jnp.stack([src, dst])
    xn = _layernorm(x, axis=-1)
    x = x + _L0_gnn_ref(xn, edge_index, edge_attr_16, L0_gnn_W1, L0_gnn_b1, L0_gnn_W2, L0_gnn_b2, L0_gnn_eps) + _L0_mix_ref(xn[None], L0_mix_Wq, L0_mix_Wkv, L0_mix_Wproj, L0_mix_bproj)[0]
    x = x + _L0_ffn_ref(_layernorm(x, axis=-1)[None], L0_ffn_W_ih, L0_ffn_W_hh, L0_ffn_b_ih, L0_ffn_b_hh, L0_ffn_W_lin, L0_ffn_b_lin, L0_ffn_fw_att, L0_ffn_bw_att)[0]
    return x

_drawn_inputs = setup_inputs


def setup_inputs(seed=0):
    import zlib

    import numpy as np

    out = dict(_drawn_inputs(seed))
    spreads = {'L0_gnn_b1': (0.0, 0.476),
     'L0_gnn_b2': (0.0, 0.33),
     'L0_mix_bproj': (0.0, 0.333),
     'L0_ffn_fw_att': (0.0010000000474974513, 0.6),
     'L0_ffn_bw_att': (0.0010000000474974513, 0.6)}
    factors = {'L0_mix_Wq': 25.632,
     'L0_mix_Wkv': 8.0,
     'L0_mix_Wproj': 8.0,
     'L0_ffn_W_hh': 3.537,
     'L0_ffn_b_ih': 8.0,
     'L0_ffn_b_hh': 8.0}
    for name, (base, spread) in spreads.items():
        noise = np.random.default_rng([zlib.crc32(name.encode()), seed]).standard_normal(out[name].shape)
        drawn = base * np.exp(spread * noise) if base else spread * noise
        out[name] = jnp.asarray(drawn.astype(out[name].dtype))
    for name, factor in factors.items():
        out[name] = (out[name] * factor).astype(out[name].dtype)
    return out
```

```python
from contextlib import ExitStack

import concourse.bass as bass
from concourse import mybir

F32 = mybir.dt.float32
BF16 = mybir.dt.bfloat16
I32 = mybir.dt.int32
ALU = mybir.AluOpType
ACT = mybir.ActivationFunctionType
AX = mybir.AxisListType.X
ds = bass.ds

P = 128
N, D = 6250, 256
E = 206250
TP = 125
NT = N // TP
BN = 250
NB = N // BN
EPS = 1e-5
XCH = 5
XT = NT // XCH

EB = 2048
EJ = EB // P
NS = -(-E // EB)
ETAIL = E - (NS - 1) * EB
WIN = 128
WSHIFT = 7

G4 = 4 * D
LS = 50
CH = N // LS
HC = 2 * CH
TOL2 = float(2.0 ** -17) ** 2

BIG = 12800


def build(nc, a, out):
    x, src, dst = a["x"], a["src"], a["dst"]
    xn_d = nc.dram_tensor("xn_rows", (N + 1, D), F32).ap()
    mix_d = nc.dram_tensor("x_plus_mix", (NB, P, 2 * BN), F32).ap()
    win_d = nc.dram_tensor("windows", (NS, 2), I32).ap()

    with ExitStack() as ctx:
        def sb(name, cols, dt=F32, parts=P):
            return ctx.enter_context(nc.sbuf_tensor(name, [parts, cols], dt))

        def sem(name):
            return ctx.enter_context(nc.semaphore(name))

        bufA, bufB, bufC = sb("bufA", BIG), sb("bufB", BIG), sb("bufC", BIG)
        x_rows = bufA[0:TP, 0:NT * D].rearrange("p (t d) -> p t d", d=D)
        xnT = bufA[:, 0:2 * N].rearrange("p (c n) -> p c n", c=2)
        ls_in = bufA[:, 0:(LS + 1) * HC].rearrange("p (t c j) -> p t c j", c=2, j=CH)
        cum = bufA[:, 0:2 * (N + 1)].rearrange("p (c n) -> p c n", c=2)
        raw_ih = bufB[:, 0:8 * D].rearrange("p (m d) -> p m d", d=D)
        raw_hh = bufB[:, 8 * D:16 * D].rearrange("p (m d) -> p m d", d=D)
        raw_q = bufB[:, 16 * D:18 * D].rearrange("p (m d) -> p m d", d=D)
        raw_kv = bufB[:, 18 * D:22 * D].rearrange("p (m d) -> p m d", d=D)
        raw_p = bufB[:, 22 * D:24 * D].rearrange("p (m d) -> p m d", d=D)
        agg = bufB[:, :].rearrange("p (c n) -> p c n", c=2)
        hs = bufB[:, 0:(LS + 1) * HC].rearrange("p (t c j) -> p t c j", c=2, j=CH)
        dst_i = bufC[0:NS, 0:EB].bitcast(I32)
        src_i = bufC[0:NS, EB:2 * EB].bitcast(I32)
        dst_f = bufC[0:NS, 2 * EB:3 * EB]
        src_f = bufC[0:NS, 3 * EB:4 * EB]
        gath = bufC[:, 0:2 * EJ * D].rearrange("p (u j d) -> p u j d", u=2, d=D)
        onehot = bufC[:, 2 * EJ * D:2 * EJ * D + EJ * WIN].rearrange("p (j w) -> p j w", w=WIN)
        x1T = bufC[:, 0:2 * N].rearrange("p (c n) -> p c n", c=2)

        wih, whh = sb("wih", 2 * G4), sb("whh", 2 * G4)
        wq, wk, wv, wp = (sb(n, 2 * D) for n in ("wq", "wk", "wv", "wp"))
        wihv, whhv = (w[:, :].rearrange("p (k o) -> p k o", k=2) for w in (wih, whh))
        wqv, wkv, wvv, wpv = (w[:, :].rearrange("p (k o) -> p k o", k=2) for w in (wq, wk, wv, wp))
        rel_buf = sb("rel_buf", EJ * NS)
        relT = rel_buf[:, :].rearrange("p (j s) -> p j s", j=EJ)
        w1v, w2v = (rel_buf[:, v * 2 * D:(v + 1) * 2 * D].rearrange("p (k o) -> p k o", k=2) for v in range(2))
        srcT = sb("srcT", EJ * NS, I32)[:, :].rearrange("p (j s) -> p j s", j=EJ)
        idx = sb("idx", 2 * EJ, I32)[:, :].rearrange("p (u j) -> p u j", u=2)

        ident = sb("ident", P)
        iota_f, pass_off = sb("iota_f", WIN), sb("pass_off", N // WIN + 2)
        ones = sb("ones", P)
        inv_d = sb("inv_d", P)
        cols = sb("cols", 16)
        eps_c, eps1 = cols[:, 0:1], cols[:, 1:2]
        b1c, b2c, bpc = cols[:, 2:4], cols[:, 4:6], cols[:, 6:8]
        fwc, bwc = cols[:, 8:10], cols[:, 10:12]
        blc = cols[:, 12:14]
        nbw, tbw = sb("nbw", 2), sb("tbw", 2)
        lin_c = sb("lin_c", 4)
        lin_rep = wih[:, 0:4 * P].rearrange("p (a m) -> p a m", a=4)
        bias_b = sb("bias_b", 3 * P, BF16, 8)[:, :].rearrange("p (a n) -> p a n", a=3)
        bias24 = sb("bias24", P, BF16, 24)
        sel24 = sb("sel24", 8 * CH, BF16, 24)

        stats = sb("stats", 6)
        mv = [sb(f"mv{v}", XT * 2) for v in range(2)]
        rstd = [sb(f"rstd{v}", XT) for v in range(2)]
        eps_ln = sb("eps_ln", 1)
        mn, mx = sb("mn", 1), sb("mx", 1)
        win_i = sb("win_i", 4, I32)
        win_row = sb("win_row", 2 * NS, I32, 1)
        sig = sb("sig", 1)
        tick = sb("tick", 8)
        ctxb = sb("ctxb", 2 * P)[:, :].rearrange("p (a n) -> p a n", a=2)
        ksb = sb("ksb", 2 * P)[:, :].rearrange("p (a n) -> p a n", a=2)
        worst, good, flag = sb("worst", 1), sb("good", 1), sb("flag", 1, I32)
        scr = sb("scr", 3072)
        bias_f = scr[0:8, 0:4 * P].rearrange("p (a n) -> p a n", a=4)
        iota_i = scr[:, 512:512 + WIN].bitcast(I32)
        pass_i = scr[:, 768:768 + N // WIN + 2].bitcast(I32)
        zrow = scr[0:1, 1024:1024 + D]
        xr_s = [scr[0:TP, u * 256:u * 256 + D] for u in range(2)]
        xt_s = [scr[:, 512 + u * 256:512 + u * 256 + 2 * TP].rearrange("p (c n) -> p c n", c=2) for u in range(2)]
        k_e, k_r = scr[0:TP, 1024:1024 + D], scr[0:TP, 1280:1280 + D]
        k_s = [scr[0:TP, 1536 + u * 256:1536 + u * 256 + D] for u in range(2)]
        MT, ksum = scr[:, 0:2 * D], scr[:, 512:512 + D]
        part = [scr[:, 512 * v:512 * v + 2 * BN].rearrange("p (c n) -> p c n", c=2) for v in range(6)]
        x2 = [scr[0:TP, 512 * v:512 * v + 2 * D].rearrange("p (t d) -> p t d", d=D) for v in (4, 5)]
        mixo, rec = scr[:, 512 * 2:512 * 2 + 2 * BN], part[0]
        y1, mixi, xc = part[0:2], part[2:4], part[4:6]
        sq = [w[:, 0:2 * BN].rearrange("p (c n) -> p c n", c=2) for w in (wq, wk)]
        sd = [wv[:, v * BN:(v + 1) * BN] for v in range(2)]
        rs = wp[:, 0:BN]
        tg_c = [scr[:, 512 * v:512 * v + 2 * HC].rearrange("p (a n) -> p a n", a=2) for v in (0, 1)]
        s_if = scr[:, 1024:1024 + 2 * HC].rearrange("p (a n) -> p a n", a=2)
        s_o, th = scr[:, 1536:1536 + HC], scr[:, 1536 + HC:1536 + 2 * HC]
        prod = scr[:, 2048:2048 + 2 * HC].rearrange("p (a n) -> p a n", a=2)
        init_c = scr[:, 2560:2560 + HC].rearrange("p (c j) -> p c j", c=2)
        dif = wk[:, 0:4 * (CH - 1)].rearrange("p (a j) -> p a j", a=4)
        lg0, gsel = [scr[:, v * BN:(v + 1) * BN] for v in range(2)], scr[:, 512:512 + BN]
        suf, res = part[2:4], part[4:6]
        outs = [w[0:TP, :].rearrange("p (t d) -> p t d", d=D) for w in (wq, wk)]

        psum = ctx.enter_context(nc.psum_tensor("psum", [P, 8, 512], F32))

        def bank(b, c=2, w=BN, parts=P):
            return psum[0:parts, b, 0:c * w].rearrange("p (c n) -> p c n", c=c)

        S = {n: sem(n) for n in (
            "ld_edges", "ld_w", "ld_w12", "ld_small", "ld_bias", "src_filled", "ident_ok", "const_ok", "const_v",
            "edge_v", "rel_ok", "win_st", "win_ok", "tr_ps", "tr_sb", "ln_v", "ln_std", "ln_r", "std_act", "eps_v", "xn_ok", "xn_st", "filled",
            "bias_v", "bias_mv", "agg_zero",
            "idx_ok", "pool_tick", "gat0", "gat1", "oh_ok", "pass_mm", "agg_v", "step_done",
            "xr_ld0", "xr_ld1", "xt_ps", "xt_agg", "xt_slot", "xt_A", "k_ps", "k_neg", "k_act", "q_neg", "k_v", "m_mm",
            "ctx_sb", "ctx_z", "ctx_ps", "ctx_v",
            "q_ps", "q_act", "q_v", "nd_ps", "nd_v", "pj_ps", "pj_act", "mix_st", "x2_ld0", "x2_ld1",
            "y1_ps", "y1_act", "mx_ld0", "mx_ld1", "y2_ps", "x1_v", "mean_ps", "xc_v", "sq_act", "var_ps", "var_v", "xs_v",
            "st_v", "g_mm", "if_mm", "o_mm", "sif_act", "so_act", "prod_v", "c_v", "th_act", "h_v",
            "sw_d", "sw_v", "cnt_mm", "flag_v",
            "pe_swept", "lin_v", "lg_mm", "lg_act", "lg_g", "lg_v", "cum_v", "suf_act", "t_v", "out_mm", "out_act", "out_st0", "out_st1")}
        ld_x = [sem(f"ld_x{q}") for q in range(XCH)]

        groups = []
        for g in range(EJ // 4):
            groups.append(([dst_f[:, (4 * g + j) * P:(4 * g + j + 1) * P] for j in range(4)], NS,
                           relT[:, 4 * g:4 * g + 4, :], "edge"))
        for g in range(EJ // 4):
            groups.append(([src_f[:, (4 * g + j) * P:(4 * g + j + 1) * P] for j in range(4)], NS,
                           srcT[:, 4 * g:4 * g + 4, :], "edge"))
        for raw, m0, w in ((raw_kv, 0, wkv), (raw_kv, 2, wvv), (raw_q, 0, wqv), (raw_p, 0, wpv)):
            groups.append(([raw[:, m0 + m, k * P:(k + 1) * P] for k in range(2) for m in range(2)], P,
                           w[:, :, :].rearrange("p k (m o) -> p (k m) o", m=2), "w"))
        for raw, w in ((raw_ih, wihv), (raw_hh, whhv)):
            for k in range(2):
                for mg in range(2):
                    groups.append(([raw[:, 4 * mg + m, k * P:(k + 1) * P] for m in range(4)], P,
                                   w[:, k, mg * 512:(mg + 1) * 512].rearrange("p (m o) -> p m o", m=4), "w"))

        def gnn_schedule(e, step):
            with e.Fori(0, NT // 2) as i:
                for u in range(2):
                    step(2 * i + u, u, "tile", 2 * i + u)
            step(None, None, "context", None)
            with e.Fori(0, (NB - 1) // 2) as i:
                for u in range(2):
                    step(NT + 2 * i + u, u, "block", 2 * i + u)
            step(NT + NB - 1, 0, "block", NB - 1)
            step(NT + NB, 1, None, None)
            with e.Fori((NT + NB + 1) // 2, (NS - 1) // 2) as i:
                for u in range(2):
                    step(2 * i + u, u, None, None)
            step(NS - 1, 0, None, None)

        def skewed(e, iteration, stages):
            first = stages + 1
            for i in range(first):
                iteration(i, i % 2)
            pairs = (NB - first) // 2
            with e.Fori(0, pairs) as r:
                for u in range(2):
                    iteration(first + 2 * r + u, (first + u) % 2, inner=True)
            for i in range(first + 2 * pairs, NB + stages - 1):
                iteration(i, i % 2)

        block = ctx.enter_context(nc.Block())

        @block.sync
        def _(sp):
            sp.dma_start(dst_i[0:NS - 1, :], dst[0:(NS - 1) * EB].rearrange("(s e) -> s e", e=EB)).then_inc(S["ld_edges"], 16)
            sp.dma_start(dst_i[NS - 1:NS, 0:ETAIL], dst[(NS - 1) * EB:E].rearrange("(s e) -> s e", s=1)).then_inc(S["ld_edges"], 16)
            sp.dma_start(dst_i[NS - 1:NS, ETAIL:EB], dst[E - (EB - ETAIL):E].rearrange("(s e) -> s e", s=1)).then_inc(S["ld_edges"], 16)
            sp.wait_ge(S["src_filled"], 1)
            sp.dma_start(src_i[0:NS - 1, :], src[0:(NS - 1) * EB].rearrange("(s e) -> s e", e=EB)).then_inc(S["ld_edges"], 16)
            sp.dma_start(src_i[NS - 1:NS, 0:ETAIL], src[(NS - 1) * EB:E].rearrange("(s e) -> s e", s=1)).then_inc(S["ld_edges"], 16)
            for q in range(XCH):
                sp.dma_start(x_rows[:, q * XT:(q + 1) * XT, :],
                             x[q * XT * TP:(q + 1) * XT * TP, :].rearrange("(t p) d -> p t d", p=TP)).then_inc(ld_x[q], 16)
            sp.wait_ge(S["edge_v"], 6)
            sp.dma_start(win_d, win_i[0:NS, 0:2]).then_inc(S["win_st"], 16)
            sp.wait_ge(S["filled"], 3)
            sp.dma_start(xn_d[N:N + 1, :], zrow[0:1, :]).then_inc(S["xn_st"], 16)
            sp.wait_ge(S["win_st"], 16)
            sp.dma_start(win_row[0:1, :], win_d.rearrange("(a s) c -> a (s c)", a=1)).then_inc(S["win_ok"], 16)
            for q in range(XCH):
                sp.wait_ge(S["xn_ok"], q + 1)
                sp.dma_start(xn_d[q * XT * TP:(q + 1) * XT * TP, :].rearrange("(t p) d -> p t d", p=TP),
                             x_rows[:, q * XT:(q + 1) * XT, :]).then_inc(S["xn_st"], 16)
            sp.wait_ge(S["bias_v"], 6)
            sp.wait_ge(S["const_ok"], 3)
            for k in range(3):
                sp.dma_start(bias24[8 * k:8 * k + 8, :], bias_b[:, k, :]).then_inc(S["bias_mv"], 16)
                if k:
                    sp.dma_start(sel24[8 * k:8 * k + 8, :], sel24[0:8, :]).then_inc(S["bias_mv"], 16)
            sp.wait_ge(S["xn_st"], 16 * (XCH + 1))

            def step(s, u, what, b):
                if what == "tile":
                    sp.wait_ge(S["m_mm"], b)
                    sp.dma_start(xr_s[u], xn_d[ds(b * TP, TP), :]).then_inc(S[f"xr_ld{u}"], 16)
                if what == "block":
                    sp.wait_ge(S["pj_ps"], b)
                    sp.dma_start(x2[u],
                                 x[ds(b * BN, BN), :].rearrange("(t p) d -> p t d", p=TP)).then_inc(S[f"x2_ld{u}"], 16)
                    sp.wait_ge(S["pj_act"], b + 1)
                    sp.dma_start(mix_d[ds(b, 1), :, :].rearrange("b p n -> p (b n)"),
                                 mixo[:, :]).then_inc(S["mix_st"], 16)
            gnn_schedule(sp, step)

            sp.wait_ge(S["step_done"], NS + 1)
            sp.dma_start(w1v, a["L0_gnn_W1"].rearrange("(k p) o -> p k o", p=P)).then_inc(S["ld_w12"], 16)
            sp.dma_start(w2v, a["L0_gnn_W2"].rearrange("(k p) o -> p k o", p=P)).then_inc(S["ld_w12"], 16)
            sp.wait_ge(S["mix_st"], 16 * NB)

            def tail(i, par, inner=False):
                if inner or i < NB:
                    if inner or i >= 2:
                        sp.wait_ge(S["x1_v"], 2 * (i - 1))
                    sp.dma_start(mixi[par], mix_d[ds(i, 1), :, :].rearrange("b p (c n) -> p (b c) n", c=2)).then_inc(S[f"mx_ld{par}"], 16)
            for i in range(2):
                tail(i, i % 2)
            with sp.Fori(1, (NB - 1) // 2) as r:
                for u in range(2):
                    tail(2 * r + u, u, inner=True)
            tail(NB - 1, 0)

            def store(i, par):
                sp.wait_ge(S["out_act"], i + 1)
                sp.dma_start(out[ds(i * BN, BN), :].rearrange("(t p) d -> p t d", p=TP), outs[par]).then_inc(S[f"out_st{par}"], 16)
            with sp.Fori(0, (NB - 1) // 2) as r:
                for u in range(2):
                    store(2 * r + u, u)
            store(NB - 1, 0)
            sp.wait_ge(S["out_st0"], 16 * ((NB + 1) // 2))
            sp.wait_ge(S["out_st1"], 16 * (NB // 2))

        @block.gpsimd
        def _(pool):
            pool.wait_ge(S["filled"], 3)
            pool.affine_select(out=ident[:, :], in_=ident[:, :], compare_op=ALU.not_equal, fill=1.0, base=0,
                               pattern=[[-1, P]], channel_multiplier=1).then_inc(S["ident_ok"], 1)
            pool.wait_ge(S["ident_ok"], 1)
            pool.iota(iota_i, [[1, WIN]], base=0, channel_multiplier=0).then_inc(S["const_ok"], 1)
            pool.wait_ge(S["const_ok"], 1)
            pool.iota(pass_i, [[WIN, N // WIN + 2]], base=0, channel_multiplier=0).then_inc(S["const_ok"], 1)
            pool.wait_ge(S["const_ok"], 2)
            pool.affine_select(out=sel24[0:8, :].rearrange("p (q j) -> p q j", q=8),
                               in_=sel24[0:8, :].rearrange("p (q j) -> p q j", q=8), compare_op=ALU.not_equal,
                               fill=1.0, base=0, pattern=[[-1, 8], [0, CH]], channel_multiplier=1).then_inc(S["const_ok"], 1)
            pool.dma_start(raw_kv, a["L0_mix_Wkv"].rearrange("(m p) d -> p m d", p=P)).then_inc(S["ld_w"], 16)
            pool.dma_start(raw_q, a["L0_mix_Wq"].rearrange("(m p) d -> p m d", p=P)).then_inc(S["ld_w"], 16)
            pool.dma_start(raw_p, a["L0_mix_Wproj"].rearrange("(m p) d -> p m d", p=P)).then_inc(S["ld_w"], 16)
            pool.dma_start(raw_ih, a["L0_ffn_W_ih"].rearrange("(m p) d -> p m d", p=P)).then_inc(S["ld_w"], 16)
            pool.dma_start(raw_hh, a["L0_ffn_W_hh"].rearrange("(m p) d -> p m d", p=P)).then_inc(S["ld_w"], 16)
            pool.dma_start(eps_c, a["L0_gnn_eps"].partition_broadcast(P)).then_inc(S["ld_small"], 16)
            pool.dma_start(blc, a["L0_ffn_b_lin"].partition_broadcast(P)).then_inc(S["ld_small"], 16)
            with nc.allow_non_contiguous_dma(reason="six vectors of 256 elements, onto the partitions"):
                for c, name in ((b1c, "L0_gnn_b1"), (b2c, "L0_gnn_b2"), (bpc, "L0_mix_bproj")):
                    pool.dma_start(c, a[name].rearrange("(m p) -> p m", p=P)).then_inc(S["ld_small"], 16)
                for c, name in ((fwc, "L0_ffn_fw_att"), (bwc, "L0_ffn_bw_att")):
                    pool.dma_start(c, a[name].rearrange("a (m p) -> p (a m)", p=P)).then_inc(S["ld_small"], 16)
                pool.dma_start(lin_c[:, :], a["L0_ffn_W_lin"].rearrange("l (k p) -> p (l k)", p=P)).then_inc(S["ld_small"], 16)
            for m in range(8):
                for k, name in enumerate(("L0_ffn_b_ih", "L0_ffn_b_hh")):
                    pool.dma_start(bias_f[m:m + 1, k, :], a[name][m * P:(m + 1) * P].rearrange("(a n) -> a n", a=1)).then_inc(S["ld_bias"], 16)

            pool.wait_ge(S["xn_st"], 16 * (XCH + 1))
            pool.wait_ge(S["tr_sb"], 2 * EJ // 4)

            def step(s, u, what, b):
                if what == "context":
                    return
                first = isinstance(s, int) and s < 2
                if not first:
                    pool.wait_ge(S["step_done"], s)
                pool.wait_ge(S["pool_tick"], s)
                pool.tensor_copy(idx[:, u, :], srcT[:, :, ds(s, 1)].rearrange("p j s -> p (j s)")).then_inc(S["idx_ok"], 1)
                pool.wait_ge(S["idx_ok"], s + 1)
                pool.tensor_tensor(tick[0:1, 0:1], ones[0:1, 0:1], ones[0:1, 0:1], ALU.add
                                   ).then_inc(S["pool_tick"], 1)
                for j in range(EJ):
                    pool.indirect_dma_start(out=gath[:, u, j, :], out_offset=None, in_=xn_d,
                                            in_offset=bass.IndirectOffsetOnAxis(ap=idx[:, u, j:j + 1], axis=0)
                                            ).then_inc(S[f"gat{u}"], 16)
            gnn_schedule(pool, step)

        @block.tensor
        def _(pe):
            mm = pe.matmul
            pe.wait_ge(S["ident_ok"], 1)
            for n, (blocks, rows, _, kind) in enumerate(groups):
                if kind == "edge":
                    pe.wait_ge(S["rel_ok"], 1 if n < EJ // 4 else 2)
                else:
                    pe.wait_ge(S["ld_w"], 80)
                if n >= 4:
                    pe.wait_ge(S["tr_sb"], n - 3)
                for j, b in enumerate(blocks):
                    last = pe.transpose(psum[:, 4 + n % 4, j * P:j * P + rows], b, ident[0:rows, 0:rows])
                last.then_inc(S["tr_ps"], 1)
            ng = len(groups)
            pe.wait_ge(S["tr_sb"], ng)
            pe.wait_ge(S["win_ok"], 16)
            pe.wait_ge(S["agg_zero"], 1)

            passes = pe.alloc_register("pe_passes")
            pe.reg_mov(passes, 0)

            def step(s, u, what, b):
                if what == "context":
                    pe.wait_ge(S["ctx_sb"], 2)
                    for h in range(2):
                        for k in range(2):
                            mm(psum[:, 2, h * P:(h + 1) * P], MT[:, k * D + h * P:k * D + (h + 1) * P],
                               wvv[:, k, h * P:(h + 1) * P], start=(k == 0), stop=(k == 1))
                        last = pe.transpose(psum[:, 3, h * P:(h + 1) * P], ksum[:, h * P:(h + 1) * P], ident[:, :])
                    last.then_inc(S["ctx_ps"], 1)
                    return
                if what == "tile":
                    pe.wait_ge(S[f"xr_ld{u}"], 8 * (b - u) + 16)
                    pe.wait_ge(S["xt_A"], b)
                    for c in range(2):
                        last = pe.transpose(bank(2 + u, 2, TP)[:, c, :], xr_s[u][:, c * P:(c + 1) * P], ident[0:TP, 0:TP])
                    last.then_inc(S["xt_ps"], 1)
                if what == "block":
                    pe.wait_ge(S["ctx_v"], 1)
                    for m in range(2):
                        for k in range(2):
                            last = mm(bank(2)[:, m, :], wqv[:, k, m * P:(m + 1) * P], xnT[:, k, ds(b * BN, BN)],
                                      start=(k == 0), stop=(k == 1))
                    last.then_inc(S["q_ps"], 1)
                pe.wait_ge(S[f"gat{u}"], 8 * EJ * (s - u) + 16 * EJ)
                n = pe.value_load(win_row[0:1, ds(s * 2 + 1, 1)], min_val=1, max_val=NT)
                p0 = pe.snap(passes)
                with pe.Fori(0, n) as k:
                    pe.wait_ge(S["oh_ok"], p0 + k + 1)
                    for h in range(2):
                        for j in range(EJ):
                            last = mm(psum[:, 0, h * WIN:(h + 1) * WIN], gath[:, u, j, h * P:(h + 1) * P],
                                      onehot[:, j, :], start=(j == 0), stop=(j == EJ - 1))
                    last.then_inc(S["pass_mm"], 1)
                pe.reg_add(passes, p0, n)
                if what == "tile":
                    pe.wait_ge(S["xt_slot"], b + 1)
                    for c in range(2):
                        last = mm(psum[0:TP, 4 + u, 0:D], xt_s[u][:, c, :], wkv[:, c, :], start=(c == 0), stop=(c == 1))
                    last.then_inc(S["k_ps"], 1)
                    pe.wait_ge(S["k_v"], b + 1)
                    for c in range(2):
                        mm(psum[:, 6, c * D:(c + 1) * D], xr_s[u][:, c * P:(c + 1) * P], k_s[u],
                           start=False, stop=False, skip_group_check=True)
                    mm(psum[:, 7, 0:D], ones[0:TP, :], k_s[u], start=False, stop=False,
                       skip_group_check=True).then_inc(S["m_mm"], 1)
                if what == "block":
                    pe.wait_ge(S["q_v"], b + 1)
                    for h in range(2):
                        mm(bank(3)[:, h, :], ctxb[:, h, :], part[2][:, h, :], start=True, stop=True)
                    for h in range(2):
                        last = mm(bank(4)[:, h, :], ksb[:, h, :], part[2][:, h, :], start=True, stop=True)
                    last.then_inc(S["nd_ps"], 1)
                    pe.wait_ge(S["nd_v"], 3 * b + 3)
                    pe.wait_ge(S[f"x2_ld{u}"], 8 * (b - u) + 16)
                    pe.wait_ge(S["pj_act"], b)
                    for m in range(2):
                        for k in range(2):
                            mm(bank(5)[:, m, :], wpv[:, k, m * P:(m + 1) * P], part[3][:, k, :],
                               start=(k == 0), stop=False, skip_group_check=True)
                        for t in range(2):
                            last = mm(bank(5)[:, m, t * TP:(t + 1) * TP], x2[u][:, t, m * P:(m + 1) * P],
                                      ident[0:TP, 0:TP], start=False, stop=(t == 1), skip_group_check=True)
                    last.then_inc(S["pj_ps"], 1)
            gnn_schedule(pe, step)

            pe.wait_ge(S["ld_w12"], 32)
            pe.wait_ge(S["step_done"], NS + 1)
            pe.wait_ge(S["const_v"], 2)

            def tail(i, par, inner=False):
                ok = lambda s: inner or 0 <= i - s < NB
                if ok(0):
                    if inner or i >= 2:
                        pe.wait_ge(S["y1_act"], 2 * i - 2)
                    for m in range(2):
                        for k in range(2):
                            last = mm(bank(par)[:, m, :], w1v[:, k, m * P:(m + 1) * P], agg[:, k, ds(i * BN, BN)],
                                      start=(k == 0), stop=(k == 1))
                    last.then_inc(S["y1_ps"], 1)
                if ok(1):
                    b, q = i - 1, 1 - par
                    pe.wait_ge(S["y1_act"], 2 * b + 2)
                    if inner or b >= 2:
                        pe.wait_ge(S["x1_v"], 2 * b - 2)
                    for m in range(2):
                        for k in range(2):
                            last = mm(bank(2 + q)[:, m, :], w2v[:, k, m * P:(m + 1) * P], y1[q][:, k, :],
                                      start=(k == 0), stop=(k == 1))
                    last.then_inc(S["y2_ps"], 1)
                if ok(2):
                    b, q = i - 2, par
                    pe.wait_ge(S["x1_v"], 2 * b + 2)
                    if inner or b >= 2:
                        pe.wait_ge(S["xc_v"], b - 1)
                    for k in range(2):
                        last = mm(psum[:, 4 + q, 0:BN], inv_d[:, :], x1T[:, k, ds(b * BN, BN)], start=(k == 0), stop=(k == 1))
                    last.then_inc(S["mean_ps"], 1)
                if ok(3):
                    b, q = i - 3, 1 - par
                    pe.wait_ge(S["sq_act"], b + 1)
                    if inner or b >= 2:
                        pe.wait_ge(S["std_act"], b - 1)
                    for k in range(2):
                        last = mm(psum[:, 6 + q, 0:BN], inv_d[:, :], sq[q][:, k, :], start=(k == 0), stop=(k == 1))
                    last.then_inc(S["var_ps"], 1)
            skewed(pe, tail, 4)

            pe.wait_ge(S["bias_mv"], 80)
            pe.wait_ge(S["xs_v"], NB + 1)
            pe.wait_ge(S["st_v"], 3)

            def gate_bank(u, m):
                return psum[:, 4 * u + m // 2, (m % 2) * CH:(m % 2 + 1) * CH]

            def prefill(t, u):
                for g in range(4):
                    mm(psum[:, 4 * u + g, 0:HC], bias24[:, :], sel24[:, g * HC:(g + 1) * HC],
                       start=True, stop=False, skip_group_check=True)
                    for m in (2 * g, 2 * g + 1):
                        for c in range(2):
                            mm(gate_bank(u, m), wihv[:, c, m * P:(m + 1) * P],
                               ls_in[:, ds(t, 1), c, :].rearrange("p t j -> p (t j)"),
                               start=False, stop=False, skip_group_check=True)

            def recur(t, u, gates, done):
                for m in gates:
                    for c in range(2):
                        last = mm(gate_bank(u, m), whhv[:, c, m * P:(m + 1) * P],
                                  hs[:, ds(t, 1), c, :].rearrange("p t j -> p (t j)"),
                                  start=False, stop=(c == 1), skip_group_check=True)
                last.then_inc(done, 1)

            prefill(0, 0)
            k_r_, go = pe.alloc_register("pe_sweeps"), pe.alloc_register("pe_go")
            pe.reg_mov(k_r_, 0)
            pe.reg_mov(go, CH)
            with pe.While(lambda: pe.snap(go) > pe.snap(k_r_)):
                kv = pe.snap(k_r_)
                base = pe.snap(kv * LS)
                with pe.Fori(0, LS // 2) as i:
                    for u in range(2):
                        t = 2 * i + u
                        done = pe.snap(base + t)
                        pe.wait_ge(S["h_v"], done)
                        recur(t, u, (4, 5), S["g_mm"])
                        recur(t, u, (0, 1, 2, 3), S["if_mm"])
                        recur(t, u, (6, 7), S["o_mm"])
                        pe.wait_ge(S["so_act"], done)
                        prefill(t + 1, 1 - u)
                pe.wait_ge(S["sw_v"], kv + 1)
                mm(psum[0:1, 4, 0:1], good[:, :], ones[:, 0:1], start=True, stop=True).then_inc(S["cnt_mm"], 1)
                pe.wait_ge(S["flag_v"], kv + 1)
                pe.reg_add(k_r_, kv, 1)
                pe.reg_mov(go, pe.value_load(flag[0:1, 0:1], min_val=0, max_val=CH))

            mm(psum[0:1, 5, 0:1], ones[:, 0:1], ones[:, 0:1], start=True, stop=True).then_inc(S["pe_swept"], 1)
            pe.wait_ge(S["lin_v"], 1)
            def logits(i, par, first):
                if not first:
                    pe.wait_ge(S["lg_g"], i - 1)
                for l in range(2):
                    for k in range(2):
                        last = mm(psum[:, 6 + par, l * BN:(l + 1) * BN], lin_rep[:, 2 * l + k, :],
                                  hs[:, ds(2 * i + 1, 2), k, :], start=(k == 0), stop=(k == 1))
                last.then_inc(S["lg_mm"], 1)
            logits(0, 0, True)
            logits(1, 1, True)
            with pe.Fori(1, (NB - 1) // 2) as r:
                for u in range(2):
                    logits(2 * r + u, u, False)
            logits(NB - 1, 0, False)

            def rows(i, par, first):
                pe.wait_ge(S["t_v"], 4 * i + 4)
                if not first:
                    pe.wait_ge(S["out_act"], i - 1)
                for t in range(2):
                    for c in range(2):
                        last = pe.transpose(psum[0:TP, par, t * D + c * P:t * D + (c + 1) * P],
                                            res[par][:, c, t * TP:(t + 1) * TP], ident[:, :])
                last.then_inc(S["out_mm"], 1)
            rows(0, 0, True)
            rows(1, 1, True)
            with pe.Fori(1, (NB - 1) // 2) as r:
                for u in range(2):
                    rows(2 * r + u, u, False)
            rows(NB - 1, 0, False)

        @block.scalar
        def _(act):
            fn = act.activation
            act.wait_ge(S["eps_v"], 1)
            for n, (blocks, rows, to, kind) in enumerate(groups):
                if n >= 8 and n % 2 == 0 and (n - 8) // 2 < XCH:
                    q = (n - 8) // 2
                    act.wait_ge(S["ln_v"], 2 * XT * (q + 1))
                    fn(rstd[q % 2][0:TP, :], mv[q % 2][0:TP, :].rearrange("p (t c) -> p t c", c=2)[:, :, 1], ACT.Sqrt,
                       bias=eps_ln[0:TP, :]).then_inc(S["ln_std"], 1)
                act.wait_ge(S["tr_ps"], n + 1)
                fn(to, psum[:, 4 + n % 4, :].rearrange("p (j n) -> p j n", j=4)[:, :, 0:rows], ACT.Copy).then_inc(S["tr_sb"], 1)
            act.wait_ge(S["ld_small"], 128)

            def elu_parts(e, r, z, negated, done, b):
                fn(e, z, ACT.Relu, scale=-1.0).then_inc(S[negated], 1)
                fn(r, z, ACT.Relu)
                act.wait_ge(S[negated], b + 1)
                fn(e, e, ACT.Exp, scale=-1.0).then_inc(S[done], 1)

            def step(s, u, what, b):
                if what == "tile":
                    act.wait_ge(S["xt_ps"], b + 1)
                    act.wait_ge(S["xt_agg"], b)
                    fn(xt_s[u], bank(2 + u, 2, TP), ACT.Copy).then_inc(S["xt_slot"], 1)
                    act.wait_ge(S["xt_slot"], b + 1)
                    fn(xnT[:, :, ds(b * TP, TP)], xt_s[u], ACT.Copy).then_inc(S["xt_A"], 1)
                    act.wait_ge(S["k_ps"], b + 1)
                    act.wait_ge(S["k_v"], b)
                    elu_parts(k_e, k_r, psum[0:TP, 4 + u, 0:D], "k_neg", "k_act", b)
                if what == "block":
                    act.wait_ge(S["q_ps"], b + 1)
                    act.wait_ge(S["q_v"], b)
                    elu_parts(part[0], part[1], bank(2), "q_neg", "q_act", b)
                    act.wait_ge(S["pj_ps"], b + 1)
                    act.wait_ge(S["mix_st"], b * 16)
                    for m in range(2):
                        last = fn(mixo[:, m * BN:(m + 1) * BN], bank(5)[:, m, :], ACT.Identity, bias=bpc[:, m:m + 1])
                    last.then_inc(S["pj_act"], 1)
            gnn_schedule(act, step)

            def tail(i, par, inner=False):
                ok = lambda s: inner or 0 <= i - s < NB
                if ok(0):
                    act.wait_ge(S["y1_ps"], i + 1)
                    if inner or i >= 2:
                        act.wait_ge(S["y2_ps"], i - 1)
                    for m in range(2):
                        fn(y1[par][:, m, :], bank(par)[:, m, :], ACT.Relu, bias=b1c[:, m:m + 1]).then_inc(S["y1_act"], 1)
                if ok(2):
                    b, q = i - 2, par
                    act.wait_ge(S["xc_v"], b + 1)
                    if inner or b >= 2:
                        act.wait_ge(S["var_ps"], b - 1)
                    fn(sq[q], xc[q], ACT.Square).then_inc(S["sq_act"], 1)
                if ok(3):
                    b, q = i - 3, 1 - par
                    act.wait_ge(S["var_ps"], b + 1)
                    if inner or b >= 2:
                        act.wait_ge(S["var_v"], b - 1)
                    fn(sd[q], psum[:, 6 + q, 0:BN], ACT.Sqrt, bias=eps_ln[:, :]).then_inc(S["std_act"], 1)
            skewed(act, tail, 4)

            act.wait_ge(S["st_v"], 3)
            k_r_, go = act.alloc_register("act_sweeps"), act.alloc_register("act_go")
            act.reg_mov(k_r_, 0)
            act.reg_mov(go, CH)
            with act.While(lambda: act.snap(go) > act.snap(k_r_)):
                kv = act.snap(k_r_)
                base = act.snap(kv * LS)
                with act.Fori(0, LS // 2) as i:
                    for u in range(2):
                        now = act.snap(base + 2 * i + u + 1)
                        act.wait_ge(S["g_mm"], now)
                        fn(tg_c[u][:, 0, :], psum[:, 4 * u + 2, 0:HC], ACT.Tanh)
                        act.wait_ge(S["if_mm"], now)
                        fn(s_if[:, :, :], psum[:, 4 * u:4 * u + 2, 0:HC], ACT.Sigmoid).then_inc(S["sif_act"], 1)
                        act.wait_ge(S["o_mm"], now)
                        fn(s_o[:, :], psum[:, 4 * u + 3, 0:HC], ACT.Sigmoid).then_inc(S["so_act"], 1)
                        act.wait_ge(S["c_v"], now)
                        fn(th[:, :], tg_c[1 - u][:, 1, :], ACT.Tanh).then_inc(S["th_act"], 1)
                act.wait_ge(S["flag_v"], kv + 1)
                act.reg_add(k_r_, kv, 1)
                act.reg_mov(go, act.value_load(flag[0:1, 0:1], min_val=0, max_val=CH))

            def logits(i, par, first):
                act.wait_ge(S["lg_mm"], i + 1)
                if not first:
                    act.wait_ge(S["lg_g"], i - 1)
                fn(lg0[par], psum[:, 6 + par, 0:BN], ACT.Identity, bias=blc[:, 0:1]).then_inc(S["lg_act"], 1)
            logits(0, 0, True)
            logits(1, 1, True)
            with act.Fori(1, (NB - 1) // 2) as r:
                for u in range(2):
                    logits(2 * r + u, u, False)
            logits(NB - 1, 0, False)

            act.wait_ge(S["cum_v"], 5)

            def results(i, par, first):
                if not first:
                    act.wait_ge(S["t_v"], 4 * i - 4)
                for c in range(2):
                    last = fn(suf[par][:, c, :], cum[:, c, ds(i * BN + 1, BN)], ACT.Identity, bias=tbw[:, c:c + 1],
                              scale=nbw[:, c:c + 1])
                last.then_inc(S["suf_act"], 1)
                act.wait_ge(S["out_mm"], i + 1)
                if not first:
                    act.wait_ge(S[f"out_st{par}"], 8 * (i - par))
                fn(outs[par], psum[0:TP, par, :].rearrange("p (t d) -> p t d", t=2), ACT.Copy).then_inc(S["out_act"], 1)
            results(0, 0, True)
            results(1, 1, True)
            with act.Fori(1, (NB - 1) // 2) as r:
                for u in range(2):
                    results(2 * r + u, u, False)
            results(NB - 1, 0, False)

        @block.vector
        def _(dve):
            tt, ts, stt = dve.tensor_tensor, dve.tensor_scalar, dve.scalar_tensor_tensor
            dve.memset(eps_ln[:, :], EPS).then_inc(S["eps_v"], 1)
            dve.memset(src_i[96:NS, :], N).then_inc(S["src_filled"], 1)
            dve.memset(ident[:, :], 0.0).then_inc(S["filled"], 1)
            dve.memset(sel24[0:8, :], 0.0).then_inc(S["filled"], 1)
            dve.memset(ones[:, :], 1.0)
            dve.memset(zrow, 0.0).then_inc(S["filled"], 1)
            dve.wait_ge(S["ld_edges"], 80)
            dve.tensor_copy(dst_f, dst_i).then_inc(S["edge_v"], 1)
            dve.wait_ge(S["edge_v"], 1)
            dve.tensor_reduce(mn[0:NS, :], dst_f, AX, ALU.min)
            dve.tensor_reduce(mx[0:NS, :], dst_f, AX, ALU.max).then_inc(S["edge_v"], 1)
            dve.wait_ge(S["edge_v"], 2)
            dve.tensor_copy(win_i[0:NS, 0:1], mn[0:NS, :]).then_inc(S["edge_v"], 1)
            tt(win_i[0:NS, 2:3], mx[0:NS, :], mn[0:NS, :], ALU.subtract).then_inc(S["edge_v"], 1)
            dve.wait_ge(S["edge_v"], 4)
            ts(win_i[0:NS, 3:4], win_i[0:NS, 2:3], WSHIFT, None, ALU.arith_shift_right).then_inc(S["edge_v"], 1)
            ts(dst_f, dst_f, mn[0:NS, 0:1], None, ALU.subtract).then_inc(S["rel_ok"], 1)
            dve.wait_ge(S["edge_v"], 5)
            ts(win_i[0:NS, 1:2], win_i[0:NS, 3:4], 1.0, None, ALU.add).then_inc(S["edge_v"], 1)
            dve.tensor_copy(src_f, src_i).then_inc(S["rel_ok"], 1)

            def row_stats(q):
                dve.wait_ge(ld_x[q], 16)
                for t in range(XT):
                    n = 2 * (q * XT + t)
                    dve.wait_ge(S["ln_v"], n)
                    dve.bn_stats(stats[0:TP, :], x_rows[:, q * XT + t, :]).then_inc(S["ln_v"], 1)
                    dve.wait_ge(S["ln_v"], n + 1)
                    dve.bn_aggr(mv[q % 2][0:TP, 2 * t:2 * t + 2], stats[0:TP, :]).then_inc(S["ln_v"], 1)

            def row_norm(q):
                dve.wait_ge(S["ln_std"], q + 1)
                dve.reciprocal(rstd[q % 2][0:TP, :], rstd[q % 2][0:TP, :]).then_inc(S["ln_r"], 1)
                dve.wait_ge(S["ln_r"], q + 1)
                for t in range(XT):
                    last = ts(x_rows[:, q * XT + t, :], x_rows[:, q * XT + t, :], mv[q % 2][0:TP, 2 * t:2 * t + 1],
                              rstd[q % 2][0:TP, t:t + 1], ALU.subtract, ALU.mult)
                last.then_inc(S["xn_ok"], 1)
                dve.wait_ge(S["xn_ok"], q + 1)

            row_stats(0)
            for q in range(XCH):
                if q + 1 < XCH:
                    row_stats(q + 1)
                row_norm(q)

            dve.wait_ge(S["const_ok"], 3)
            dve.wait_ge(S["ld_small"], 128)
            dve.tensor_copy(iota_f[:, :], iota_i[:, :])
            dve.tensor_copy(pass_off[:, :], pass_i[:, :])
            dve.memset(inv_d[:, :], 1.0 / D)
            ts(eps1, eps_c, 1.0, None, ALU.add).then_inc(S["const_v"], 1)
            ts(nbw[:, :], bwc, -1.0, None, ALU.mult).then_inc(S["const_v"], 1)
            dve.wait_ge(S["const_v"], 2)
            dve.wait_ge(S["ld_bias"], 256)
            tt(bias_f[:, 2, :], bias_f[:, 0, :], bias_f[:, 1, :], ALU.add).then_inc(S["bias_v"], 1)
            dve.wait_ge(S["bias_v"], 1)
            dve.tensor_copy(bias_b[:, 0, :], bias_f[:, 2, :]).then_inc(S["bias_v"], 1)
            dve.wait_ge(S["bias_v"], 2)
            tt(bias_f[:, 3, :], bias_f[:, 2, :], bias_b[:, 0, :], ALU.subtract).then_inc(S["bias_v"], 1)
            dve.wait_ge(S["bias_v"], 3)
            dve.tensor_copy(bias_b[:, 1, :], bias_f[:, 3, :]).then_inc(S["bias_v"], 1)
            dve.wait_ge(S["bias_v"], 4)
            tt(bias_f[:, 2, :], bias_f[:, 3, :], bias_b[:, 1, :], ALU.subtract).then_inc(S["bias_v"], 1)
            dve.wait_ge(S["bias_v"], 5)
            dve.tensor_copy(bias_b[:, 2, :], bias_f[:, 2, :]).then_inc(S["bias_v"], 1)

            dve.wait_ge(S["tr_sb"], len(groups))
            dve.memset(psum[:, 6:8, :], 0.0)
            dve.memset(bufB[:, :], 0.0).then_inc(S["agg_zero"], 1)
            dve.wait_ge(S["agg_zero"], 1)
            dve.wait_ge(S["win_ok"], 16)
            passes = dve.alloc_register("dve_passes")
            dve.reg_mov(passes, 0)

            def step(s, u, what, b):
                if what == "context":
                    dve.wait_ge(S["m_mm"], NT)
                    dve.tensor_copy(MT[:, :], psum[:, 6, :]).then_inc(S["ctx_sb"], 1)
                    dve.tensor_copy(ksum[:, :], psum[:, 7, 0:D]).then_inc(S["ctx_sb"], 1)
                    dve.memset(ctxb[:, :, :], 0.0).then_inc(S["ctx_z"], 1)
                    dve.memset(ksb[:, :, :], 0.0).then_inc(S["ctx_z"], 1)
                    dve.wait_ge(S["ctx_z"], 2)
                    dve.wait_ge(S["ctx_ps"], 1)
                    for h in range(2):
                        for g in range(4):
                            q = slice(32 * g, 32 * g + 32)
                            dve.tensor_copy(ctxb[q, h, q], psum[q, 2, h * P + 32 * g:h * P + 32 * g + 32])
                            last = dve.tensor_copy(ksb[q, h, q], psum[q, 3, h * P + 32 * g:h * P + 32 * g + 32])
                    last.then_inc(S["ctx_v"], 1)
                    return
                base = dve.value_load(win_row[0:1, ds(s * 2, 1)], min_val=0, max_val=N - 1)
                n = dve.value_load(win_row[0:1, ds(s * 2 + 1, 1)], min_val=1, max_val=NT)
                p0 = dve.snap(passes)
                with dve.Fori(0, n) as k:
                    dve.wait_ge(S["pass_mm"], p0 + k)
                    stt(onehot, relT[:, :, ds(s, 1)].broadcast_to([P, EJ, WIN]), pass_off[:, ds(k, 1)],
                        iota_f[:, :].unsqueeze(1).broadcast_to([P, EJ, WIN]), ALU.subtract, ALU.is_equal).then_inc(S["oh_ok"], 1)
                    dve.wait_ge(S["pass_mm"], p0 + k + 1)
                    at = nc.s_assert_within(base + k * WIN, 0, N - 1,
                                            skip_runtime_bounds_check_because="it is at most the largest of dst")
                    w = agg[:, :, ds(at, WIN)]
                    tt(w, psum[:, 0, 0:2 * WIN].rearrange("p (c w) -> p c w", c=2), w, ALU.add).then_inc(S["agg_v"], 1)
                    dve.wait_ge(S["agg_v"], p0 + k + 1)
                dve.reg_add(passes, p0, n)
                dve.wait_ge(S["step_done"], s + 1)
                dve.memset(tick[0:1, 2:3], 0.0).then_inc(S["step_done"], 1)
                if what == "tile":
                    dve.wait_ge(S["xt_slot"], b + 1)
                    w = agg[:, :, ds(b * TP, TP)]
                    stt(w, xt_s[u], eps1, w, ALU.mult, ALU.add).then_inc(S["xt_agg"], 1)
                    dve.wait_ge(S["k_act"], b + 1)
                    tt(k_s[u], k_e, k_r, ALU.add).then_inc(S["k_v"], 1)
                    dve.wait_ge(S["xt_agg"], b + 2)
                if what == "block":
                    dve.wait_ge(S["q_act"], b + 1)
                    dve.wait_ge(S["mix_st"], b * 16)
                    tt(part[2], part[0], part[1], ALU.add).then_inc(S["q_v"], 1)
                    dve.wait_ge(S["nd_ps"], b + 1)
                    ts(rec, bank(4), 1e-6, None, ALU.max).then_inc(S["nd_v"], 1)
                    dve.wait_ge(S["nd_v"], 3 * b + 1)
                    dve.reciprocal(rec, rec).then_inc(S["nd_v"], 1)
                    dve.wait_ge(S["nd_v"], 3 * b + 2)
                    tt(part[3], bank(3), rec, ALU.mult).then_inc(S["nd_v"], 1)
            dve.memset(tick[0:1, 3:4], 0.0).then_inc(S["xt_agg"], 1)
            dve.memset(tick[0:1, 4:5], 0.0).then_inc(S["xt_A"], 1)
            dve.memset(tick[0:1, 5:6], 0.0).then_inc(S["step_done"], 1)
            gnn_schedule(dve, step)

            def tail(i, par, inner=False):
                ok = lambda s: inner or 0 <= i - s < NB
                if ok(1):
                    b, q = i - 1, 1 - par
                    dve.wait_ge(S["y2_ps"], b + 1)
                    dve.wait_ge(S[f"mx_ld{q}"], 8 * (b - q) + 16)
                    for m in range(2):
                        stt(x1T[:, m, ds(b * BN, BN)], bank(2 + q)[:, m, :], b2c[:, m:m + 1], mixi[q][:, m, :],
                            ALU.add, ALU.add).then_inc(S["x1_v"], 1)
                if ok(2):
                    b, q = i - 2, par
                    dve.wait_ge(S["mean_ps"], b + 1)
                    if inner or b >= 2:
                        dve.wait_ge(S["xs_v"], b - 1)
                        dve.wait_ge(S["sq_act"], b - 1)
                    tt(xc[q], x1T[:, :, ds(b * BN, BN)], psum[:, 4 + q, 0:BN].unsqueeze(1).broadcast_to([P, 2, BN]),
                       ALU.subtract).then_inc(S["xc_v"], 1)
                if ok(3):
                    b, q = i - 3, 1 - par
                    dve.wait_ge(S["std_act"], b + 1)
                    dve.reciprocal(rs, sd[q]).then_inc(S["var_v"], 1)
                    dve.wait_ge(S["var_v"], b + 1)
                    for c in range(2):
                        last = tt(ls_in[:, 0:LS, c, ds(b * (BN // LS), BN // LS)].rearrange("p t j -> p j t"),
                                  xc[q][:, c, :].rearrange("p (j t) -> p j t", t=LS),
                                  rs.rearrange("p (j t) -> p j t", t=LS), ALU.mult)
                    last.then_inc(S["xs_v"], 1)
                    dve.wait_ge(S["xs_v"], b + 1)
            skewed(dve, tail, 4)
            dve.tensor_copy(ls_in[:, LS, :, :], ls_in[:, 0, :, :]).then_inc(S["xs_v"], 1)

            dve.wait_ge(S["y1_ps"], NB)
            dve.memset(hs[:, 0, :, :], 0.0).then_inc(S["st_v"], 1)
            dve.wait_ge(S["xs_v"], NB)
            dve.wait_ge(S["var_ps"], NB)
            dve.memset(init_c[:, :, :], 0.0).then_inc(S["st_v"], 1)
            dve.memset(tg_c[0][:, 1, :], 0.0).then_inc(S["st_v"], 1)
            dve.wait_ge(S["st_v"], 3)
            k_r_, go = dve.alloc_register("dve_sweeps"), dve.alloc_register("dve_go")
            dve.reg_mov(k_r_, 0)
            dve.reg_mov(go, CH)
            with dve.While(lambda: dve.snap(go) > dve.snap(k_r_)):
                kv = dve.snap(k_r_)
                base = dve.snap(kv * LS)
                with dve.Fori(0, LS // 2) as i:
                    for u in range(2):
                        now = dve.snap(base + 2 * i + u + 1)
                        dve.wait_ge(S["sif_act"], now)
                        tt(prod[:, :, :], s_if[:, :, :], tg_c[u][:, :, :], ALU.mult).then_inc(S["prod_v"], 1)
                        dve.wait_ge(S["prod_v"], now)
                        tt(tg_c[1 - u][:, 1, :], prod[:, 0, :], prod[:, 1, :], ALU.add).then_inc(S["c_v"], 1)
                        dve.wait_ge(S["th_act"], now)
                        tt(hs[:, ds(2 * i + u + 1, 1), :, :].rearrange("p t c j -> p (t c j)"), s_o[:, :], th[:, :],
                           ALU.mult).then_inc(S["h_v"], 1)
                dve.wait_ge(S["h_v"], base + LS)
                cN = tg_c[0][:, 1, :].rearrange("p (c j) -> p c j", c=2)
                tt(dif[:, 0:2, :], hs[:, LS, :, 0:CH - 1], hs[:, 0, :, 1:CH], ALU.subtract)
                tt(dif[:, 2:4, :], cN[:, :, 0:CH - 1], init_c[:, :, 1:CH], ALU.subtract).then_inc(S["sw_d"], 1)
                dve.wait_ge(S["sw_d"], kv * 6 + 1)
                tt(dif[:, :, :], dif[:, :, :], dif[:, :, :], ALU.mult).then_inc(S["sw_d"], 1)
                dve.tensor_copy(init_c[:, :, 1:CH], cN[:, :, 0:CH - 1]).then_inc(S["sw_d"], 1)
                dve.tensor_copy(hs[:, 0, :, 1:CH], hs[:, LS, :, 0:CH - 1]).then_inc(S["sw_d"], 1)
                dve.wait_ge(S["sw_d"], kv * 6 + 4)
                dve.tensor_reduce(worst[:, :], dif[:, :, :].rearrange("p a j -> p (a j)"), AX, ALU.max).then_inc(S["sw_d"], 1)
                dve.tensor_copy(cN, init_c[:, :, :]).then_inc(S["sw_d"], 1)
                dve.wait_ge(S["sw_d"], kv * 6 + 6)
                ts(good[:, :], worst[:, :], TOL2, None, ALU.is_le).then_inc(S["sw_v"], 1)
                dve.wait_ge(S["cnt_mm"], kv + 1)
                ts(flag[0:1, :], psum[0:1, 4, 0:1], P - 0.5, float(CH), ALU.is_lt, ALU.mult).then_inc(S["flag_v"], 1)
                dve.wait_ge(S["flag_v"], kv + 1)
                dve.reg_add(k_r_, kv, 1)
                dve.reg_mov(go, dve.value_load(flag[0:1, 0:1], min_val=0, max_val=CH))

            dve.wait_ge(S["pe_swept"], 1)
            dve.tensor_copy(lin_rep, lin_c[:, :].unsqueeze(2).broadcast_to([P, 4, P])).then_inc(S["lin_v"], 1)
            dve.memset(cum[:, :, 0:1], 0.0).then_inc(S["cum_v"], 1)

            def gate(i, par, first):
                dve.wait_ge(S["lg_act"], i + 1)
                stt(gsel[:, :], psum[:, 6 + par, BN:2 * BN], blc[:, 1:2], lg0[par], ALU.add, ALU.is_gt).then_inc(S["lg_g"], 1)
                dve.wait_ge(S["lg_g"], i + 1)
                for c in range(2):
                    last = tt(cum[:, c, 1:N + 1].rearrange("p (j t) -> p t j", t=LS)[:, ds(2 * i, 2), :],
                              hs[:, ds(2 * i + 1, 2), c, :], gsel[:, :].rearrange("p (t j) -> p t j", t=2), ALU.mult)
                last.then_inc(S["lg_v"], 1)
                dve.wait_ge(S["lg_v"], i + 1)
            with dve.Fori(0, (NB - 1) // 2) as r:
                for u in range(2):
                    gate(2 * r + u, u, False)
            gate(NB - 1, 0, False)
            for c in range(2):
                dve.tensor_tensor_scan(cum[:, c, 1:N + 1], ones[:, 0:1].broadcast_to([P, N]), cum[:, c, 1:N + 1], 0.0,
                                       ALU.mult, ALU.add).then_inc(S["cum_v"], 1)
            dve.wait_ge(S["cum_v"], 3)
            for c in range(2):
                ts(tbw[:, c:c + 1], cum[:, c, N:N + 1], bwc[:, c:c + 1], None, ALU.mult).then_inc(S["cum_v"], 1)

            def results(i, par, first):
                if not first:
                    dve.wait_ge(S["out_mm"], i - 1)
                for c in range(2):
                    last = stt(res[par][:, c, :].rearrange("p (j t) -> p j t", t=LS),
                               hs[:, 1:LS + 1, c, ds(i * (BN // LS), BN // LS)].rearrange("p t j -> p j t"), 2.0,
                               x1T[:, c, ds(i * BN, BN)].rearrange("p (j t) -> p j t", t=LS), ALU.mult, ALU.add)
                last.then_inc(S["t_v"], 1)
                dve.wait_ge(S["t_v"], 4 * i + 1)
                for c in range(2):
                    stt(res[par][:, c, :], cum[:, c, ds(i * BN, BN)], fwc[:, c:c + 1], res[par][:, c, :],
                        ALU.mult, ALU.add).then_inc(S["t_v"], 1)
                dve.wait_ge(S["t_v"], 4 * i + 3)
                dve.wait_ge(S["suf_act"], i + 1)
                tt(res[par], res[par], suf[par], ALU.add).then_inc(S["t_v"], 1)
            results(0, 0, True)
            results(1, 1, True)
            with dve.Fori(1, (NB - 1) // 2) as r:
                for u in range(2):
                    results(2 * r + u, u, False)
            results(NB - 1, 0, False)


_INS = ["x", "src", "dst", "L0_gnn_W1", "L0_gnn_b1", "L0_gnn_W2", "L0_gnn_b2", "L0_gnn_eps",
        "L0_mix_Wq", "L0_mix_Wkv", "L0_mix_Wproj", "L0_mix_bproj", "L0_ffn_W_ih", "L0_ffn_W_hh", "L0_ffn_b_ih",
        "L0_ffn_b_hh", "L0_ffn_W_lin", "L0_ffn_b_lin", "L0_ffn_fw_att", "L0_ffn_bw_att"]


def kernel(**inputs):
    import numpy as _np
    import concourse.bacc as _bacc
    from concourse import mybir as _mybir
    from concourse.bass_utils import run_bass_kernel_spmd as _run

    nc = _bacc.Bacc("TRN2", target_bir_lowering=False, num_devices=1)
    arrays, aps = {}, {}
    for name in _INS:
        v = _np.ascontiguousarray(inputs[name])
        arrays[f"in_{name}_dram"] = v
        aps[name] = nc.dram_tensor(f"in_{name}_dram", v.shape, _mybir.dt.from_np(v.dtype), kind="ExternalInput").ap()
    out = nc.dram_tensor("out_0_dram", (N, D), _mybir.dt.float32, kind="ExternalOutput").ap()
    build(nc, aps, out)
    r = _run(nc, [arrays], core_ids=[0])
    return r.results[0]["out_0_dram"]
```
